# Optimizing a Trainium2 kernel written in Bass

```python
import numpy as np
import jax
import jax.numpy as jnp

def _softmax(x, axis=-1):
    return jax.nn.softmax(x, axis=axis)

def _gelu(x):
    return jax.nn.gelu(x, approximate=True)

def _silu(x):
    return jax.nn.silu(x)

def _sigmoid(x):
    return jax.nn.sigmoid(x)

def _layernorm(x, axis=-1, eps=1e-05):
    m = jnp.mean(x, axis=axis, keepdims=True)
    v = jnp.var(x, axis=axis, keepdims=True)
    return (x - m) / jnp.sqrt(v + eps)

def _scatter_add(tgt, idx, src, axis=0):
    return tgt.at[idx].add(src)

def _segment_sum(src, seg, n):
    return jax.ops.segment_sum(src, seg, n)
kernel_name = 'mk_adj_resnorm_d4_adj_r2_48a199'

def setup_inputs(seed: int=0):
    np.random.seed(seed)
    _w = jnp.asarray

    def _rec_inputs():
        import jax
        import jax.numpy as jnp
        _gk = jax.random.key(seed)
        x = -0.003407 + 1.001 * jax.random.normal(jax.random.fold_in(_gk, 1), (8, 1024, 64), jnp.float32)
        _w = (1.0 + jnp.arange(1024, dtype=jnp.float32)) ** (-0.5)
        _w = _w / _w.mean()
        _pij = jnp.clip(0.0078125 * _w[:, None] * _w[None, :], 0.0, 1.0)
        _a = jax.random.uniform(jax.random.fold_in(_gk, 2), (8, 1024, 1024)) < _pij
        adj = _a.astype(jnp.int32)
        return (x, adj)
    x, adj = _rec_inputs()

    def _L0_gnn_setup():
        import jax, jax.numpy as jnp
        import numpy as np
        NEG_INF = -1e+22
        key = jax.random.key(seed)
        k1, k2, k3, k4 = jax.random.split(key, 4)
        B, T, C, O = (2, 512, 64, 64)
        feat = jax.random.normal(k1, (B, T, C), dtype=jnp.float32)
        adj = jax.random.randint(k2, (B, T, T), 0, 2, dtype=jnp.int32)
        W1 = jax.random.normal(k3, (O, 2 * C), dtype=jnp.float32) * (2 * C) ** (-0.5)
        W2 = jax.random.normal(k4, (O,), dtype=jnp.float32) * O ** (-0.5)
        return {'feat': feat, 'adj': adj, 'W1': W1, 'W2': W2}
    _L0_gnn_all = _L0_gnn_setup()
    _L0_gnn_in = {k: v for k, v in _L0_gnn_all.items() if k in ('W1', 'W2')}
    del _L0_gnn_all

    def _L1_gnn_setup():
        import jax, jax.numpy as jnp
        import numpy as np
        SLOPE = 0.2

        def act(x):
            return jax.nn.leaky_relu(x, negative_slope=SLOPE)

        def _xavier(k, shape):
            fan_in, fan_out = (shape[0], shape[1])
            lim = float(np.sqrt(6.0 / (fan_in + fan_out)))
            return jax.random.uniform(k, shape, jnp.float32, -lim, lim)
        key = jax.random.key(seed)
        ks = jax.random.split(key, 8)
        B, N, C = (2, 512, 64)
        edge_attr = jax.random.normal(ks[0], (B, N, C), jnp.float32)
        edge_adj = jax.random.randint(ks[1], (B, N, N), 0, 2).astype(jnp.int32)
        U2 = _xavier(ks[2], (C, C))
        W2 = _xavier(ks[3], (C, C))
        yita = _xavier(ks[4], (C, 1))
        beta = _xavier(ks[5], (1, 1))
        linW = _xavier(ks[6], (C, C))
        linb = jax.random.uniform(ks[7], (C,), jnp.float32, -0.1, 0.1)
        return dict(edge_attr=edge_attr, edge_adj=edge_adj, e_max=1, U2=U2, W2=W2, yita=yita, beta=beta, linW=linW, linb=linb)
    _L1_gnn_all = _L1_gnn_setup()
    _L1_gnn_in = {k: v for k, v in _L1_gnn_all.items() if k in ('U2', 'W2', 'yita', 'beta', 'linW', 'linb')}
    del _L1_gnn_all

    def _L2_gnn_setup():
        import jax, jax.numpy as jnp
        import numpy as np
        NEG_BIG = -9000000000000000.0
        key = jax.random.key(seed)
        ks = jax.random.split(key, 6)
        B, N, C, F = (4, 2048, 64, 64)
        x = jax.random.normal(ks[0], (B, N, C), dtype=jnp.float32)
        adj = jax.random.randint(ks[1], (B, N, N), 0, 2, dtype=jnp.int32)
        W1 = jax.random.normal(ks[2], (C, F), dtype=jnp.float32) * (1.0 / np.sqrt(C))
        b1 = jnp.zeros((F,), dtype=jnp.float32)
        a1 = jax.random.normal(ks[3], (F,), dtype=jnp.float32) * (1.0 / np.sqrt(F))
        ba1 = jnp.zeros((1,), dtype=jnp.float32)
        a2 = jax.random.normal(ks[4], (F,), dtype=jnp.float32) * (1.0 / np.sqrt(F))
        ba2 = jnp.zeros((1,), dtype=jnp.float32)
        return {'x': x, 'adj': adj, 'W1': W1, 'b1': b1, 'a1': a1, 'ba1': ba1, 'a2': a2, 'ba2': ba2}
    _L2_gnn_all = _L2_gnn_setup()
    _L2_gnn_in = {k: v for k, v in _L2_gnn_all.items() if k in ('W1', 'b1', 'a1', 'ba1', 'a2', 'ba2')}
    del _L2_gnn_all

    def _L3_gnn_setup():
        import jax, jax.numpy as jnp
        import numpy as np
        B, M, D, H, NBT = (128, 128, 64, 8, 5)
        NEG_SLOPE = 0.2
        key = jax.random.key(seed)
        ks = jax.random.split(key, 10)
        s = 1.0 / np.sqrt(D)
        sp = 1.0 / np.sqrt(D * H)
        return {'atom_embeddings': jax.random.normal(ks[0], (B, M, D), dtype=jnp.float32), 'edges': jax.random.randint(ks[1], (B, M, M), 0, NBT, dtype=jnp.int32), 'Wq': jax.random.normal(ks[2], (D, D * H), dtype=jnp.float32) * s, 'bq': jnp.zeros((D * H,), dtype=jnp.float32), 'Wk': jax.random.normal(ks[3], (D, D * H), dtype=jnp.float32) * s, 'bk': jnp.zeros((D * H,), dtype=jnp.float32), 'Wv': jax.random.normal(ks[4], (D, D * H), dtype=jnp.float32) * s, 'bv': jnp.zeros((D * H,), dtype=jnp.float32), 'edge_bias': jax.random.normal(ks[5], (NBT, H), dtype=jnp.float32) * 0.1, 'Wp': jax.random.normal(ks[6], (D * H, D), dtype=jnp.float32) * sp, 'bp': jnp.zeros((D,), dtype=jnp.float32)}
    _L3_gnn_all = _L3_gnn_setup()
    _L3_gnn_in = {k: v for k, v in _L3_gnn_all.items() if k in ('Wq', 'bq', 'Wk', 'bk', 'Wv', 'bv', 'edge_bias', 'Wp', 'bp')}
    del _L3_gnn_all
    return {'x': x, 'adj': adj, 'L0_gnn_W1': _L0_gnn_in['W1'], 'L0_gnn_W2': _L0_gnn_in['W2'], 'L1_gnn_U2': _L1_gnn_in['U2'], 'L1_gnn_W2': _L1_gnn_in['W2'], 'L1_gnn_yita': _L1_gnn_in['yita'], 'L1_gnn_beta': _L1_gnn_in['beta'], 'L1_gnn_linW': _L1_gnn_in['linW'], 'L1_gnn_linb': _L1_gnn_in['linb'], 'L2_gnn_W1': _L2_gnn_in['W1'], 'L2_gnn_b1': _L2_gnn_in['b1'], 'L2_gnn_a1': _L2_gnn_in['a1'], 'L2_gnn_ba1': _L2_gnn_in['ba1'], 'L2_gnn_a2': _L2_gnn_in['a2'], 'L2_gnn_ba2': _L2_gnn_in['ba2'], 'L3_gnn_Wq': _L3_gnn_in['Wq'], 'L3_gnn_bq': _L3_gnn_in['bq'], 'L3_gnn_Wk': _L3_gnn_in['Wk'], 'L3_gnn_bk': _L3_gnn_in['bk'], 'L3_gnn_Wv': _L3_gnn_in['Wv'], 'L3_gnn_bv': _L3_gnn_in['bv'], 'L3_gnn_edge_bias': _L3_gnn_in['edge_bias'], 'L3_gnn_Wp': _L3_gnn_in['Wp'], 'L3_gnn_bp': _L3_gnn_in['bp']}

def reference(x, adj, L0_gnn_W1, L0_gnn_W2, L1_gnn_U2, L1_gnn_W2, L1_gnn_yita, L1_gnn_beta, L1_gnn_linW, L1_gnn_linb, L2_gnn_W1, L2_gnn_b1, L2_gnn_a1, L2_gnn_ba1, L2_gnn_a2, L2_gnn_ba2, L3_gnn_Wq, L3_gnn_bq, L3_gnn_Wk, L3_gnn_bk, L3_gnn_Wv, L3_gnn_bv, L3_gnn_edge_bias, L3_gnn_Wp, L3_gnn_bp):
    import jax
    import jax.numpy as jnp

    def _L0_gnn_ref(feat, adj, W1, W2):
        import jax, jax.numpy as jnp
        import numpy as np
        NEG_INF = -1e+22
        C = feat.shape[-1]
        W1a, W1b = (W1[:, :C], W1[:, C:])
        fa = jnp.einsum('btc,oc->bto', feat, W1a)
        fb = jnp.einsum('btc,oc->bto', feat, W1b)
        h = jax.nn.relu(fa[:, :, None, :] + fb[:, None, :, :])
        att = jnp.einsum('bijo,o->bij', h, W2)
        mask = jnp.where(adj > 0, 0.0, NEG_INF).astype(att.dtype)
        att = jax.nn.softmax(att + mask, axis=-1)
        return jnp.einsum('bij,bjc->bic', att, feat)

    def _L1_gnn_ref(edge_attr, edge_adj, e_max, U2, W2, yita, beta, linW, linb):
        import jax, jax.numpy as jnp
        import numpy as np
        SLOPE = 0.2

        def act(x):
            return jax.nn.leaky_relu(x, negative_slope=SLOPE)

        def _xavier(k, shape):
            fan_in, fan_out = (shape[0], shape[1])
            lim = float(np.sqrt(6.0 / (fan_in + fan_out)))
            return jax.random.uniform(k, shape, jnp.float32, -lim, lim)
        vu = edge_attr @ U2
        iv = edge_attr @ W2
        lr = act(vu[:, :, None, :] + iv[:, None, :, :])
        scores = jnp.einsum('bijc,c->bij', lr, yita[:, 0])
        scores = jnp.where(edge_adj > 0, scores, jnp.float32(-1000000000000.0))
        alpha = jax.nn.softmax(scores, axis=2)
        agg = act(jnp.einsum('bij,bjc->bic', alpha, edge_attr))
        emb = act((agg + (1.0 + beta[0, 0]) * edge_attr) @ linW.T + linb)
        return emb

    def _L2_gnn_ref(x, adj, W1, b1, a1, ba1, a2, ba2):
        import jax, jax.numpy as jnp
        import numpy as np
        NEG_BIG = -9000000000000000.0
        seq_fts = jnp.einsum('bnc,cf->bnf', x, W1) + b1
        f1 = seq_fts @ a1 + ba1[0]
        f2 = seq_fts @ a2 + ba2[0]
        logits = f1[:, None, :] + f2[:, :, None]
        logits = jax.nn.leaky_relu(logits, negative_slope=0.01)
        attention = jnp.where(adj > 0, logits, jnp.float32(NEG_BIG))
        coefs = jax.nn.softmax(attention, axis=1)
        ret = jnp.einsum('bij,bjf->bif', coefs, seq_fts)
        return jax.nn.elu(ret)

    def _L3_gnn_ref(atom_embeddings, edges, Wq, bq, Wk, bk, Wv, bv, edge_bias, Wp, bp):
        import jax, jax.numpy as jnp
        import numpy as np
        B, M, D, H, NBT = (128, 128, 64, 8, 5)
        NEG_SLOPE = 0.2
        b, m, d = atom_embeddings.shape
        h = edge_bias.shape[1]
        q = (atom_embeddings @ Wq + bq).reshape(b, m, h, d)
        k = (atom_embeddings @ Wk + bk).reshape(b, m, h, d)
        v = (atom_embeddings @ Wv + bv).reshape(b, m, h, d)
        scale = 1.0 / jnp.sqrt(jnp.asarray(d, dtype=q.dtype))
        scores = jnp.einsum('bmhd,bnhd->bhmn', q, k) * scale
        scores = scores + jnp.transpose(edge_bias[edges], (0, 3, 1, 2))
        scores = jax.nn.leaky_relu(scores, NEG_SLOPE)
        mask = (edges > 0)[:, None, :, :]
        scores = jnp.where(mask, scores, jnp.asarray(-1000000000.0, dtype=scores.dtype))
        attn = jax.nn.softmax(scores, axis=-1)
        out = jnp.einsum('bhmn,bnhd->bmhd', attn, v).reshape(b, m, h * d)
        return out @ Wp + bp
    x = _layernorm(x + _L0_gnn_ref(x, adj, L0_gnn_W1, L0_gnn_W2), axis=-1)
    x = _layernorm(x + _L1_gnn_ref(x, adj, 1, L1_gnn_U2, L1_gnn_W2, L1_gnn_yita, L1_gnn_beta, L1_gnn_linW, L1_gnn_linb), axis=-1)
    x = _layernorm(x + _L2_gnn_ref(x, adj, L2_gnn_W1, L2_gnn_b1, L2_gnn_a1, L2_gnn_ba1, L2_gnn_a2, L2_gnn_ba2), axis=-1)
    x = _layernorm(x + _L3_gnn_ref(x, adj, L3_gnn_Wq, L3_gnn_bq, L3_gnn_Wk, L3_gnn_bk, L3_gnn_Wv, L3_gnn_bv, L3_gnn_edge_bias, L3_gnn_Wp, L3_gnn_bp), axis=-1)
    return x

_drawn_inputs = setup_inputs


def setup_inputs(seed=0):
    import zlib

    import numpy as np

    out = dict(_drawn_inputs(seed))
    spreads = {'L2_gnn_b1': (0.0, 0.1),
     'L3_gnn_bq': (0.0, 0.324),
     'L3_gnn_bk': (0.0, 0.783),
     'L3_gnn_bv': (0.0, 0.1),
     'L3_gnn_bp': (0.0, 0.1)}
    factors = {'L3_gnn_edge_bias': 3.896}
    for name, (base, spread) in spreads.items():
        noise = np.random.default_rng([zlib.crc32(name.encode()), seed]).standard_normal(out[name].shape)
        drawn = base * np.exp(spread * noise) if base else spread * noise
        out[name] = jnp.asarray(drawn.astype(out[name].dtype))
    for name, factor in factors.items():
        out[name] = (out[name] * factor).astype(out[name].dtype)
    return out
```

```python
import numpy as np
from contextlib import ExitStack

import concourse.bass as bass
from concourse import mybir

F32 = mybir.dt.float32
BF16 = mybir.dt.bfloat16
I32 = mybir.dt.int32
ALU = mybir.AluOpType
ACT = mybir.ActivationFunctionType

P = 128
C = 64
HALF = 512
NEG = -1.0e30
LOWEST = -3.0e38
EPS = 1e-5
GAT_SLOPE = 0.2
L2_SLOPE = 0.01

GROUPS = 16
SLOTS = 4


def act_share(g):
    return (3,) if g % 2 == 0 else (2, 3)


ACT_PER_TILE = sum(len(act_share(g)) for g in range(GROUPS))
DVE_PER_TILE = 4 * GROUPS - ACT_PER_TILE


def act_made(g):
    return sum(len(act_share(i)) for i in range(g + 1))


def dve_made(g):
    return 4 * (g + 1) - act_made(g)


def project_nodes(nc, src, dst, lin, w_a, w_b, w_t, X, B2, A2, TB, work, ident, nb, n):
    tiles = n // P
    xs = work[:, 0:tiles * C]
    xT = work[0:C, 1024:1024 + n]
    with ExitStack() as ctx:
        sem = lambda s: ctx.enter_context(nc.semaphore(s))
        pX = ctx.enter_context(nc.psum_tensor(f"{lin}pX", [C, n], F32))
        pB = ctx.enter_context(nc.psum_tensor(f"{lin}pB", [P, n], F32))
        pA = ctx.enter_context(nc.psum_tensor(f"{lin}pA", [P, n // 2], F32))
        pT = ctx.enter_context(nc.psum_tensor(f"{lin}pT", [P, n], F32))
        staged, transposed, xT_ready = sem(f"{lin}staged"), sem(f"{lin}transposed"), sem(f"{lin}xT_ready")
        b_made, a_made, t_made = sem(f"{lin}b_made"), sem(f"{lin}a_made"), sem(f"{lin}t_made")
        b_out, a_out, t_out = sem(f"{lin}b_out"), sem(f"{lin}a_out"), sem(f"{lin}t_out")
        block = ctx.enter_context(nc.Block())

        @block.scalar
        def _(act):
            with act.Fori(0, nb) as b:
                act.wait_ge(transposed, b)
                act.activation(xs, X[:, bass.ds(b * tiles * C, tiles * C)], ACT.Copy).then_inc(staged, 1)
                act.wait_ge(b_made, b + 1)
                act.activation(B2[:, bass.ds(b * n, n)], pB[:, :], ACT.Copy).then_inc(b_out, 1)
                if w_t is not None:
                    act.wait_ge(t_made, b + 1)
                    act.activation(TB[:, bass.ds(b * n, n)], pT[:, :], ACT.Copy).then_inc(t_out, 1)

        @block.vector
        def _(dve):
            with dve.Fori(0, nb) as b:
                dve.wait_ge(transposed, b + 1)
                dve.wait_ge(a_made, b)
                dve.tensor_copy(xT, pX[:, :]).then_inc(xT_ready, 1)
                dve.wait_ge(a_made, b + 1)
                dve.tensor_copy(A2[:, bass.ds(b * (n // 2), n // 2)], pA[:, :]).then_inc(a_out, 1)

        @block.tensor
        def _(pe):
            with pe.Fori(0, nb) as b:
                pe.wait_ge(staged, b + 1)
                pe.wait_ge(xT_ready, b)
                pe.nop(nofuse=True)
                for t in range(tiles):
                    last = pe.transpose(pX[:, t * P:(t + 1) * P], xs[:, t * C:(t + 1) * C], ident)
                last.then_inc(transposed, 1)
                pe.wait_ge(xT_ready, b + 1)
                pe.wait_ge(b_out, b)
                for h in range(n // HALF):
                    last = pe.matmul(pB[:, h * HALF:(h + 1) * HALF], w_b, xT[:, h * HALF:(h + 1) * HALF],
                                     start=True, stop=True)
                last.then_inc(b_made, 1)
                pe.wait_ge(a_out, b)
                for odd in range(2):
                    last = pe.matmul(pA[:, :], w_a[:, odd, :], xT[:, odd:n:2], start=odd == 0, stop=odd == 1)
                last.then_inc(a_made, 1)
                if w_t is not None:
                    pe.wait_ge(b_out, b + 1)
                    pe.wait_ge(t_out, b)
                    for h in range(n // HALF):
                        last = pe.matmul(pT[:, h * HALF:(h + 1) * HALF], w_t,
                                         B2[0:C, bass.ds(b * n + h * HALF, HALF)], start=True, stop=True)
                    last.then_inc(t_made, 1)


def additive_attention(nc, name, adj, X, XN, B2, A2, TB, w_sel, hidden, adj_in, mask, Z, PT, small, ident,
                       lin, nb, n):
    tiles = n // P
    T = nb * tiles
    rows = n // 2
    with ExitStack() as ctx:
        sem = lambda s: ctx.enter_context(nc.semaphore(name + s))
        psS = [ctx.enter_context(nc.psum_tensor(f"{name}psS{i}", [P, n], F32)) for i in range(2)]
        psT = ctx.enter_context(nc.psum_tensor(f"{name}psT", [P, n], F32))
        psO = ctx.enter_context(nc.psum_tensor(f"{name}psO", [P, HALF], F32))
        psU = ctx.enter_context(nc.psum_tensor(f"{name}psU", [P, HALF], F32))
        adj_loaded = [sem(f"adj_loaded{i}") for i in range(2)]
        mask_raw, mask_used = sem("mask_raw"), sem("mask_used")
        mask_ready = sem("mask_ready") if TB is not None else mask_raw
        hid_dve, hid_act, hid_used = sem("hid_dve"), sem("hid_act"), sem("hid_used")
        max_ready, probs_ready, probs_turned = sem("max_ready"), sem("probs_ready"), sem("probs_turned")
        turned_act, turned_dve = sem("turned_act"), sem("turned_dve")
        agg_ready, u_ready, u_turned, uT_ready, lin_ready = (
            sem("agg_ready"), sem("u_ready"), sem("u_turned"), sem("uT_ready"), sem("lin_ready"))
        dve_step, var_ready, eps_added, rstd_ready = sem("dve_step"), sem("var_ready"), sem("eps_added"), sem("rstd_ready")
        x_written = sem("x_written")

        mx, negm, den, rden = (small[:, i:i + 1] for i in range(4))
        mv, vare, rstd, halfc = small[:, 4:6], small[:, 6:7], small[:, 7:8], small[:, 8:9]
        stats = small[:, 10:16]
        agg, y, uT = small[:, 64:128], small[:, 128:192], small[0:C, 192:320]

        def xt(k):
            return X[:, bass.ds(k * C, C)]

        block = ctx.enter_context(nc.Block())

        @block.sync
        def _(sp):
            def load(k, slot):
                sp.dma_start(adj_in[:, slot, :], adj[bass.ds(k * P, P), :]).then_inc(adj_loaded[slot], 16)
            load(0, 0)
            load(1, 1)
            with sp.Fori(1, T // 2) as m:
                for slot in range(2):
                    sp.wait_ge(mask_raw, 2 * m + slot - 1)
                    load(2 * m + slot, slot)

        @block.gpsimd
        def _(gp):
            def make_mask(k, m, slot, first):
                gp.wait_ge(adj_loaded[slot], 16 * m + 16)
                if not first:
                    gp.wait_ge(mask_used, k - 1)
                gp.nop(nofuse=True)
                gp.tensor_scalar(mask[:, slot, :], adj_in[:, slot, :], 0.0, NEG,
                                 ALU.is_le, ALU.mult).then_inc(mask_raw, 1)
                if TB is not None:
                    gp.wait_ge(mask_raw, k + 1)
                    gp.tensor_tensor(mask[:, slot, :], mask[:, slot, :],
                                     TB[:, bass.ds((k // tiles) * n, n)], ALU.add).then_inc(mask_ready, 1)

            def inverse_deviation(k):
                gp.wait_ge(var_ready, k + 1)
                gp.nop(nofuse=True)
                gp.tensor_scalar(vare, mv[:, 1:2], EPS, 1.0, ALU.add, ALU.mult).then_inc(eps_added, 1)
                gp.wait_ge(eps_added, k + 1)
                gp.tensor_tensor(rstd, vare, halfc, ALU.pow).then_inc(rstd_ready, 1)

            make_mask(0, 0, 0, True)
            make_mask(1, 0, 1, True)
            inverse_deviation(0)
            with gp.Fori(1, T // 2) as m:
                for slot in range(2):
                    make_mask(2 * m + slot, m, slot, False)
                    inverse_deviation(2 * m + slot - 1)
            inverse_deviation(T - 1)

        @block.scalar
        def _(act):
            def hidden_units(k, first):
                made = 0
                for g in range(GROUPS):
                    for q in act_share(g):
                        if not (first and g < SLOTS) and q == act_share(g)[0]:
                            act.wait_ge(hid_used, k * GROUPS + g - SLOTS + 1)
                        pair = (k // tiles) * rows + (k % tiles) * (P // 2) + GROUPS * q + g
                        act.activation(hidden[:, g % SLOTS, q, :], B2[:, bass.ds((k // tiles) * n, n)], ACT.Relu,
                                       bias=A2[:, bass.ds(pair, 1)]).then_inc(hid_act, 1)
                        made += 1
                    yield g

            def exponentials(k):
                act.wait_ge(max_ready, k + 1)
                act.activation(Z[:, :], Z[:, :], ACT.Exp, bias=negm, accum_out=den).then_inc(probs_ready, 1)

            def copy_turned(k):
                act.wait_ge(probs_turned, k + 1)
                act.wait_ge(agg_ready, k)
                act.activation(PT[:, 0:HALF], psT[:, 0:HALF], ACT.Copy).then_inc(turned_act, 1)

            def copy_u(k):
                act.wait_ge(u_turned, k + 1)
                act.activation(uT, psU[0:C, 0:P], ACT.Copy).then_inc(uT_ready, 1)

            posts = {5: exponentials, 8: copy_turned}
            if lin is not None:
                posts[13] = copy_u

            def tile(k, first, post):
                for g in hidden_units(k, first):
                    if post and g in posts:
                        posts[g](k - 1)

            tile(0, True, False)
            tile(1, False, True)
            with act.Fori(1, T // 2) as m:
                for slot in range(2):
                    tile(2 * m + slot, False, True)
            for g in sorted(posts):
                posts[g](T - 1)

        @block.vector
        def _(dve):
            steps = 3 if lin is None else 7

            def hidden_units(k, first):
                for g in range(GROUPS):
                    if not (first and g < SLOTS):
                        dve.wait_ge(hid_used, k * GROUPS + g - SLOTS + 1)
                    for q in range(4):
                        if q in act_share(g):
                            continue
                        pair = (k // tiles) * rows + (k % tiles) * (P // 2) + GROUPS * q + g
                        dve.tensor_scalar(hidden[:, g % SLOTS, q, :], B2[:, bass.ds((k // tiles) * n, n)],
                                          A2[:, bass.ds(pair, 1)], 0.0, ALU.add, ALU.max).then_inc(hid_dve, 1)
                    yield g

            def masked_max(k, par):
                dve.wait_ge(hid_used, (k + 1) * GROUPS)
                dve.wait_ge(mask_ready, k + 1)
                dve.wait_ge(probs_turned, k)
                dve.nop(nofuse=True)
                dve.tensor_tensor_reduce(out=Z[:, :], in0=psS[par][:, :], in1=mask[:, par, :], scale=1.0,
                                         scalar=LOWEST, op0=ALU.add, op1=ALU.max, accum_out=mx).then_inc(mask_used, 1)
                dve.wait_ge(mask_used, k + 1)
                dve.wait_ge(probs_ready, k)
                dve.tensor_scalar(negm, mx, -1.0, None, ALU.mult).then_inc(max_ready, 1)

            def copy_turned(k, par):
                dve.wait_ge(probs_turned, k + 1)
                dve.tensor_copy(PT[:, HALF:n], psT[:, HALF:n]).then_inc(turned_dve, 1)

            def step(k, i, ins):
                ins.then_inc(dve_step, 1)
                dve.wait_ge(dve_step, k * steps + i + 1)

            def norm_in(k, i):
                step(k, i, dve.bn_stats(stats, y))
                dve.nop(nofuse=True)
                dve.bn_aggr(mv, stats).then_inc(var_ready, 1)

            def layer_norm(k, par):
                dve.wait_ge(rstd_ready, k + 1)
                dve.tensor_scalar(XN[:, bass.ds(k * C, C)], y, mv[:, 0:1], rstd,
                                  ALU.subtract, ALU.mult).then_inc(x_written, 1)

            def weighted_plain(k, par):
                dve.wait_ge(agg_ready, k + 1)
                dve.wait_ge(x_written, k)
                step(k, 0, dve.reciprocal(rden, den))
                step(k, 1, dve.scalar_tensor_tensor(out=y, in0=psO[:, 0:C], scalar=rden, in1=xt(k),
                                                    op0=ALU.mult, op1=ALU.add))
                norm_in(k, 2)

            def weighted_lin(k, par):
                dve.wait_ge(agg_ready, k + 1)
                step(k, 0, dve.reciprocal(rden, den))
                step(k, 1, dve.tensor_scalar(agg, psO[:, 0:C], rden, None, ALU.mult))
                step(k, 2, dve.scalar_tensor_tensor(out=agg, in0=agg, scalar=GAT_SLOPE, in1=agg,
                                                    op0=ALU.mult, op1=ALU.max))
                dve.scalar_tensor_tensor(out=agg, in0=xt(k), scalar=lin["beta1"], in1=agg,
                                         op0=ALU.mult, op1=ALU.add).then_inc(u_ready, 1)

            def after_lin(k, par):
                dve.wait_ge(lin_ready, k + 1)
                dve.wait_ge(x_written, k)
                step(k, 3, dve.tensor_tensor(y, psU[:, P:P + C], lin["bias"], ALU.add))
                step(k, 4, dve.scalar_tensor_tensor(out=y, in0=y, scalar=GAT_SLOPE, in1=y,
                                                    op0=ALU.mult, op1=ALU.max))
                step(k, 5, dve.tensor_tensor(y, y, xt(k), ALU.add))
                norm_in(k, 6)

            if lin is None:
                posts = {3: masked_max, 8: copy_turned, 12: weighted_plain, 14: layer_norm}
            else:
                posts = {3: masked_max, 8: copy_turned, 11: weighted_lin, 14: after_lin, 15: layer_norm}

            def tile(k, first, post, par):
                for g in hidden_units(k, first):
                    if post and g in posts:
                        posts[g](k - 1, 1 - par)

            tile(0, True, False, 0)
            tile(1, False, True, 1)
            with dve.Fori(1, T // 2) as m:
                for slot in range(2):
                    tile(2 * m + slot, False, True, slot)
            for g in sorted(posts):
                posts[g](T - 1, 1)

        @block.tensor
        def _(pe):
            def turn(k):
                pe.wait_ge(probs_ready, k + 1)
                pe.wait_ge(turned_act, k)
                pe.wait_ge(turned_dve, k)
                pe.nop(nofuse=True)
                for j in range(tiles):
                    last = pe.transpose(psT[:, j * P:(j + 1) * P], Z[:, j * P:(j + 1) * P], ident)
                last.then_inc(probs_turned, 1)

            def weigh(k):
                pe.wait_ge(turned_act, k + 1)
                pe.wait_ge(turned_dve, k + 1)
                pe.wait_ge(x_written, k)
                for j in range(tiles):
                    last = pe.matmul(psO[:, 0:C], PT[:, j * P:(j + 1) * P],
                                     X[:, bass.ds(((k // tiles) * tiles + j) * C, C)],
                                     start=j == 0, stop=j == tiles - 1)
                last.then_inc(agg_ready, 1)

            def turn_u(k):
                pe.wait_ge(u_ready, k + 1)
                pe.nop(nofuse=True)
                pe.transpose(psU[0:C, 0:P], agg, ident).then_inc(u_turned, 1)

            def linear(k):
                pe.wait_ge(uT_ready, k + 1)
                pe.nop(nofuse=True)
                pe.matmul(psU[:, P:P + C], uT, lin["w"], start=True, stop=True).then_inc(lin_ready, 1)

            posts = {3: turn, 7: weigh}
            if lin is not None:
                posts[9] = turn_u
                posts[11] = linear

            def tile(k, par, first, post):
                if not first:
                    pe.wait_ge(mask_used, k - 1)
                for g in range(GROUPS):
                    pe.wait_ge(hid_dve, k * DVE_PER_TILE + dve_made(g))
                    pe.wait_ge(hid_act, k * ACT_PER_TILE + act_made(g))
                    for h in range(n // HALF):
                        for q in range(4):
                            last = pe.matmul(psS[par][32 * q:32 * q + 32, h * HALF:(h + 1) * HALF],
                                             w_sel[:, 30 - 2 * g:62 - 2 * g],
                                             hidden[:, g % SLOTS, q, h * HALF:(h + 1) * HALF],
                                             start=g == 0, stop=g == GROUPS - 1)
                    last.then_inc(hid_used, 1)
                    if post and g in posts:
                        posts[g](k - 1)

            tile(0, 0, True, False)
            tile(1, 1, True, True)
            with pe.Fori(1, T // 2) as m:
                for slot in range(2):
                    tile(2 * m + slot, slot, False, True)
            for g in sorted(posts):
                posts[g](T - 1)


HEADS = 8
PAIRS = HEADS // 2
EDGE_TYPES = 5


def multi_head_attention(nc, adj, out, w, X, buf, ident, nb, n):
    tiles = n // P
    STEPS = tiles * HEADS
    BODY = 2 * HEADS
    UNITS = STEPS // 2
    K, V, Q, xs, xT = buf["K"], buf["V"], buf["Q"], buf["xs"], buf["xT"]
    adj_in, maskf, biased, Z, PT = buf["adj_in"], buf["maskf"], buf["biased"], buf["Z"], buf["PT"]
    rinv, R, OT, y, yn = buf["rinv"], buf["R"], buf["OT"], buf["y"], buf["yn"]
    small = buf["small"]
    mx = lambda k: small[:, 16 + k % 8:17 + k % 8]
    negm = lambda k: small[:, 24 + k % 8:25 + k % 8]
    den = lambda k: small[:, 32 + k % 8:33 + k % 8]
    low = lambda k: small[:, 40 + k % 8:41 + k % 8]
    mv, vare, rstd, halfc, stats = small[:, 4:6], small[:, 6:7], small[:, 7:8], small[:, 8:9], small[:, 10:16]
    with ExitStack() as ctx:
        sem = lambda s: ctx.enter_context(nc.semaphore("m3" + s))
        psS = [ctx.enter_context(nc.psum_tensor(f"m3S{i}", [P, n], F32)) for i in range(2)]
        psT = ctx.enter_context(nc.psum_tensor("m3T", [P, n], F32))
        psO = ctx.enter_context(nc.psum_tensor("m3O", [P, HALF], F32))
        psQ = ctx.enter_context(nc.psum_tensor("m3Q", [P, PAIRS, P], F32))
        psR, psY = psQ[:, 0, :], psQ[:, 1, 0:C]
        staged, x_turned, xT_ready, k_made, k_out, v_made, v_out = (
            sem("staged"), sem("x_turned"), sem("xT_ready"), sem("k_made"), sem("k_out"), sem("v_made"), sem("v_out"))
        adj_loaded = [sem(f"adj_loaded{i}") for i in range(2)]
        mask_ready, bias_ready = sem("mask_ready"), sem("bias_ready")
        q_made, q_ready, scored, max_ready, low_ready, leaky_ready = (
            sem("q_made"), sem("q_ready"), sem("scored"), sem("max_ready"), sem("low_ready"), sem("leaky_ready"))
        probs_ready, turned, copied, weighed = sem("probs_ready"), sem("turned"), sem("copied"), sem("weighed")
        inverted, inv_ready, normed, r_ready, o_ready = (
            sem("inverted"), sem("inv_ready"), sem("normed"), sem("r_ready"), sem("o_ready"))
        projected, y_step, var_ready, eps_added, rstd_ready, y_ready = (
            sem("projected"), sem("y_step"), sem("var_ready"), sem("eps_added"), sem("rstd_ready"), sem("y_ready"))
        stored = [sem(f"stored{i}") for i in range(2)]
        block = ctx.enter_context(nc.Block())

        def pipeline(eng, stages):
            deepest = max(lag for lag, _, _, _ in stages)
            bodies = STEPS // BODY

            def at(d, s, first, tail):
                for lag, every, phase, what in stages:
                    i = s - lag
                    if tail and i >= 0:
                        continue
                    if i >= 0:
                        dd, ss = d, i
                    elif first:
                        continue
                    else:
                        dd, ss = d - 1, i + BODY
                    if every == 1 or ss % every == phase:
                        what(dd, ss)
            for s in range(BODY):
                at(0, s, True, False)
            with eng.Fori(1, bodies) as d:
                for s in range(BODY):
                    at(d, s, False, False)
            for s in range(deepest):
                at(bodies, s, False, True)

        def before(b, per_batch, d, per_body, i, back):
            if isinstance(d, int):
                return b * per_batch + min(max(d * per_body + i - back, 0), per_batch)
            return b * per_batch + d * per_body + (i - back)

        @block.sync
        def _(sp):
            with sp.Fori(0, nb) as b:
                def load(d, s):
                    t = s // HEADS
                    sp.wait_ge(bias_ready, before(b, STEPS, d, BODY, s, HEADS))
                    sp.dma_start(adj_in[:, t, :], adj[bass.ds((b * tiles + d * 2 + t) * P, P), :]
                                 ).then_inc(adj_loaded[t], 16)

                def store(d, s):
                    t = s // HEADS
                    sp.wait_ge(y_ready, before(b, tiles, d, 2, t + 1, 0))
                    sp.dma_start(out[bass.ds((b * tiles + d * 2 + t) * P, P), :], yn[:, t, :]).then_inc(stored[t], 16)
                pipeline(sp, [(0, HEADS, 0, load), (13, HEADS, HEADS - 1, store)])
            for t in range(2):
                sp.wait_ge(stored[t], 16 * nb * tiles // 2)

        @block.gpsimd
        def _(gp):
            with gp.Fori(0, nb) as b:
                def make_mask(d, s):
                    t = s // HEADS
                    gp.wait_ge(adj_loaded[t], before(b, 8 * tiles, d, 16, 16, 0))
                    gp.wait_ge(bias_ready, before(b, STEPS, d, BODY, s, 0))
                    gp.nop(nofuse=True)
                    gp.tensor_scalar(maskf[:, :], adj_in[:, t, :], 0.0, NEG, ALU.is_le, ALU.mult).then_inc(mask_ready, 1)
                    gp.wait_ge(mask_ready, before(b, tiles, d, 2, t + 1, 0))

                def add_bias(d, s):
                    gp.wait_ge(max_ready, before(b, STEPS, d, BODY, s, 1))
                    gp.nop(nofuse=True)
                    h = s % HEADS
                    gp.tensor_scalar(biased[:, s % 2, :], maskf[:, :], w["edge8"][:, h:h + 1], 1.0,
                                     ALU.add, ALU.mult).then_inc(bias_ready, 1)

                def inverse_deviation(d, s):
                    k = before(b, tiles, d, 2, s // HEADS + 1, 0)
                    gp.wait_ge(var_ready, k)
                    gp.nop(nofuse=True)
                    gp.tensor_scalar(vare, mv[:, 1:2], EPS, 1.0, ALU.add, ALU.mult).then_inc(eps_added, 1)
                    gp.wait_ge(eps_added, k)
                    gp.tensor_tensor(rstd, vare, halfc, ALU.pow).then_inc(rstd_ready, 1)
                pipeline(gp, [(0, HEADS, 0, make_mask), (0, 1, 0, add_bias), (12, HEADS, HEADS - 1, inverse_deviation)])

        @block.tensor
        def _(pe):
            with pe.Fori(0, nb) as b:
                pe.wait_ge(staged, b + 1)
                pe.wait_ge(copied, b * STEPS)
                pe.nop(nofuse=True)
                for t in range(tiles):
                    last = pe.transpose(psT[0:C, t * P:(t + 1) * P], xs[:, t * C:(t + 1) * C], ident)
                last.then_inc(x_turned, 1)
                pe.wait_ge(xT_ready, b + 1)
                pe.wait_ge(max_ready, b * STEPS)

                def keys(h):
                    if h >= 2:
                        pe.wait_ge(k_out, b * PAIRS + h - 1)
                    for half in range(n // HALF):
                        last = pe.matmul(psS[h % 2][:, half * HALF:(half + 1) * HALF], w["Wk"][:, h * P:(h + 1) * P],
                                         xT[:, half * HALF:(half + 1) * HALF], start=True, stop=True)
                    last.then_inc(k_made, 1)

                def values(j):
                    if j >= 2:
                        pe.wait_ge(v_out, b * tiles + j - 1)
                    pe.matmul(psT[:, (j % 2) * HALF:(j % 2 + 1) * HALF], xT[:, j * P:(j + 1) * P], w["Wv"],
                              start=True, stop=True).then_inc(v_made, 1)

                for h in range(PAIRS):
                    keys(h)
                    for j in range(h * tiles // PAIRS, (h + 1) * tiles // PAIRS):
                        values(j)

                def queries(d, s):
                    t = s // HEADS
                    pe.wait_ge(q_ready, before(b, tiles, d, 2, t, 0))
                    pe.wait_ge(r_ready, before(b, UNITS, d, BODY // 2, 4 * t, 3))
                    pe.wait_ge(y_step, before(b, 3 * tiles, d, 6, 3 * t, 6))
                    for h in range(PAIRS):
                        last = pe.matmul(psQ[:, h, :], w["Wq"][:, h * P:(h + 1) * P],
                                         xT[:, bass.ds((d * 2 + t) * P, P)], start=True, stop=True)
                    last.then_inc(q_made, 1)

                def scores(d, s):
                    t, h, e = s // HEADS, s % HEADS // 2, s % 2
                    if s % HEADS == 0:
                        pe.wait_ge(q_ready, before(b, tiles, d, 2, t + 1, 0))
                    if isinstance(d, int) and d == 0 and s == 0:
                        pe.wait_ge(k_out, b * PAIRS + PAIRS)
                    pe.wait_ge(max_ready, before(b, STEPS, d, BODY, s, 1))
                    rows = slice(C * e, C * e + C)
                    for half in range(n // HALF):
                        last = pe.matmul(psS[e][:, half * HALF:(half + 1) * HALF], Q[rows, t, h, :],
                                         K[rows, h, half * HALF:(half + 1) * HALF], start=True, stop=True)
                    last.then_inc(scored, 1)

                def turn(d, s):
                    pe.wait_ge(probs_ready, before(b, STEPS, d, BODY, s + 1, 0))
                    pe.wait_ge(copied, before(b, STEPS, d, BODY, s, 0))
                    if isinstance(d, int) and d == 0 and s == 0:
                        pe.wait_ge(v_out, b * tiles + tiles)
                    pe.nop(nofuse=True)
                    for j in range(tiles):
                        last = pe.transpose(psT[:, j * P:(j + 1) * P], Z[:, s % 4, j * P:(j + 1) * P], ident)
                    last.then_inc(turned, 1)

                def weigh(d, s):
                    h, u = s % HEADS // 2, s // 2
                    pe.wait_ge(copied, before(b, STEPS, d, BODY, s + 1, 0))
                    pe.wait_ge(o_ready, before(b, UNITS, d, BODY // 2, u, 0))
                    for j in range(tiles):
                        for e in range(2):
                            last = pe.matmul(psO[C * e:C * e + C, 0:P], V[:, j, (2 * h + e) * C:(2 * h + e + 1) * C],
                                             PT[:, (s - 1 + e) % 4, j * P:(j + 1) * P],
                                             start=j == 0, stop=j == tiles - 1)
                    last.then_inc(weighed, 1)

                def norm(d, s):
                    u = s // 2
                    pe.wait_ge(inv_ready, before(b, UNITS, d, BODY // 2, u + 1, 0))
                    pe.wait_ge(r_ready, before(b, UNITS, d, BODY // 2, u, 0))
                    pe.wait_ge(q_ready, before(b, tiles, d, 2, (s + 6) // 8 + 1, 0))
                    pe.wait_ge(y_step, before(b, 3 * tiles, d, 6, 3 * ((s - 13) // 8 + 1), 0))
                    pe.matmul(psR, rinv[:, u % 2, :], ident, start=True, stop=True).then_inc(normed, 1)

                def project(d, s):
                    t = s // HEADS
                    pe.wait_ge(o_ready, before(b, UNITS, d, BODY // 2, s // 2 + 1, 0))
                    pe.wait_ge(y_step, before(b, 3 * tiles, d, 6, 3 * t, 0))
                    pe.wait_ge(r_ready, before(b, UNITS, d, BODY // 2, 4 * t + 6, 0))
                    pe.wait_ge(q_ready, before(b, tiles, d, 2, t + 3, 0))
                    for h in range(PAIRS):
                        last = pe.matmul(psY, OT[:, t, h, :], w["Wp"][:, h, :],
                                         start=h == 0, stop=h == PAIRS - 1)
                    last.then_inc(projected, 1)
                pipeline(pe, [(6, 2, 1, norm), (0, HEADS, 0, queries), (1, 1, 0, scores), (3, 1, 0, turn),
                              (5, 2, 1, weigh), (11, HEADS, HEADS - 1, project)])

        @block.scalar
        def _(act):
            with act.Fori(0, nb) as b:
                act.wait_ge(x_turned, b)
                act.activation(xs, X[:, bass.ds(b * tiles * C, tiles * C)], ACT.Copy).then_inc(staged, 1)
                for h in range(PAIRS):
                    act.wait_ge(k_made, b * PAIRS + h + 1)
                    act.activation(K[:, h, :], psS[h % 2][:, :], ACT.Identity, bias=w["bk"][:, h:h + 1]).then_inc(k_out, 1)

                def exponentials(d, s):
                    act.wait_ge(leaky_ready, before(b, STEPS, d, BODY, s + 1, 0))
                    act.wait_ge(inverted, before(b, UNITS, d, BODY // 2, s // 2, 3))
                    act.activation(Z[:, s % 4, :], Z[:, s % 4, :], ACT.Exp, bias=negm(s),
                                   accum_out=den(s)).then_inc(probs_ready, 1)

                def copy_turned(d, s):
                    act.wait_ge(turned, before(b, STEPS, d, BODY, s + 1, 0))
                    act.wait_ge(weighed, before(b, UNITS, d, BODY // 2, s // 2, 1))
                    act.activation(PT[:, s % 4, :], psT[:, :], ACT.Copy).then_inc(copied, 1)

                def copy_norm(d, s):
                    u = s // 2
                    act.wait_ge(normed, before(b, UNITS, d, BODY // 2, u + 1, 0))
                    act.wait_ge(o_ready, before(b, UNITS, d, BODY // 2, u, 0))
                    act.activation(R, psR, ACT.Copy).then_inc(r_ready, 1)
                pipeline(act, [(6, 2, 1, copy_norm), (2, 1, 0, exponentials), (3, 1, 0, copy_turned)])

        @block.vector
        def _(dve):
            with dve.Fori(0, nb) as b:
                dve.wait_ge(x_turned, b + 1)
                dve.tensor_copy(xT, psT[0:C, :]).then_inc(xT_ready, 1)
                for j in range(tiles):
                    dve.wait_ge(v_made, b * tiles + j + 1)
                    dve.tensor_tensor(V[:, j, :], psT[:, (j % 2) * HALF:(j % 2 + 1) * HALF], w["bv"],
                                      ALU.add).then_inc(v_out, 1)

                def copy_queries(d, s):
                    t = s // HEADS
                    dve.wait_ge(q_made, before(b, tiles, d, 2, t + 1, 0))
                    dve.wait_ge(scored, before(b, STEPS, d, BODY, s, HEADS))
                    dve.tensor_tensor(Q[:, t, :, :], psQ[:, :, :], w["bq"].to_broadcast([P, PAIRS, P]),
                                      ALU.add).then_inc(q_ready, 1)

                def masked_leaky(d, s):
                    k1 = before(b, STEPS, d, BODY, s + 1, 0)
                    dve.wait_ge(scored, k1)
                    dve.wait_ge(bias_ready, k1)
                    dve.wait_ge(turned, before(b, STEPS, d, BODY, s, 3))
                    dve.nop(nofuse=True)
                    dve.tensor_tensor_reduce(out=Z[:, s % 4, :], in0=psS[s % 2][:, :], in1=biased[:, s % 2, :],
                                             scale=w["scale"], scalar=LOWEST, op0=ALU.add, op1=ALU.max,
                                             accum_out=mx(s)).then_inc(max_ready, 1)
                    dve.wait_ge(max_ready, k1)
                    dve.tensor_scalar(low(s), mx(s), -GAT_SLOPE, None, ALU.mult).then_inc(low_ready, 1)
                    dve.wait_ge(low_ready, k1)
                    dve.scalar_tensor_tensor(out=negm(s), in0=mx(s), scalar=-1.0, in1=low(s),
                                             op0=ALU.mult, op1=ALU.min)
                    dve.scalar_tensor_tensor(out=Z[:, s % 4, :], in0=Z[:, s % 4, :], scalar=GAT_SLOPE,
                                             in1=Z[:, s % 4, :], op0=ALU.mult, op1=ALU.max).then_inc(leaky_ready, 1)

                def invert(d, s):
                    u = s // 2
                    dve.wait_ge(probs_ready, before(b, STEPS, d, BODY, s + 1, 0))
                    dve.wait_ge(normed, before(b, UNITS, d, BODY // 2, u, 1))
                    at = 32 + (s - 1) % 8
                    dve.reciprocal(buf["rd"][:, u % 2, :], small[:, at:at + 2]).then_inc(inverted, 1)
                    dve.wait_ge(inverted, before(b, UNITS, d, BODY // 2, u + 1, 0))
                    dve.tensor_copy(rinv[:, u % 2, :].rearrange("p (e c) -> p e c", c=C),
                                    buf["rd"][:, u % 2, :].rearrange("p (e o) -> p e o", o=1).to_broadcast([P, 2, C])
                                    ).then_inc(inv_ready, 1)

                def normalise(d, s):
                    t, h, u = s // HEADS, s % HEADS // 2, s // 2
                    dve.wait_ge(r_ready, before(b, UNITS, d, BODY // 2, u + 1, 0))
                    dve.wait_ge(weighed, before(b, UNITS, d, BODY // 2, u + 1, 0))
                    dve.wait_ge(projected, before(b, tiles, d, 2, t, 1))
                    dve.tensor_tensor(OT[:, t, h, :], psO[:, 0:P], R, ALU.mult).then_inc(o_ready, 1)

                def norm_in(d, s):
                    t = s // HEADS
                    y1 = before(b, 3 * tiles, d, 6, 3 * t + 1, 0)
                    dve.wait_ge(projected, before(b, tiles, d, 2, t + 1, 0))
                    dve.tensor_tensor(y, psY, w["bp"], ALU.add).then_inc(y_step, 1)
                    dve.wait_ge(y_step, y1)
                    dve.tensor_tensor(y, y, X[:, bass.ds((b * tiles + d * 2 + t) * C, C)], ALU.add).then_inc(y_step, 1)
                    dve.wait_ge(y_step, y1 + 1)
                    dve.bn_stats(stats, y).then_inc(y_step, 1)
                    dve.wait_ge(y_step, y1 + 2)
                    dve.nop(nofuse=True)
                    dve.bn_aggr(mv, stats).then_inc(var_ready, 1)

                def norm_out(d, s):
                    t = s // HEADS
                    dve.wait_ge(rstd_ready, before(b, tiles, d, 2, t + 1, 0))
                    dve.wait_ge(stored[t], before(b, 8 * tiles, d, 16, 0, 0))
                    dve.tensor_scalar(yn[:, t, :], y, mv[:, 0:1], rstd, ALU.subtract, ALU.mult).then_inc(y_ready, 1)
                pipeline(dve, [(7, 2, 1, normalise), (0, HEADS, 0, copy_queries), (11, HEADS, HEADS - 1, norm_in),
                               (13, HEADS, HEADS - 1, norm_out), (5, 2, 1, invert), (1, 1, 0, masked_leaky)])


def load_constants(nc, ins, loads, zeros, ident, identb, small):
    with ExitStack() as ctx:
        sem = lambda s: ctx.enter_context(nc.semaphore(s))
        loaded, zeroed, made = sem("weights_loaded"), sem("weights_zeroed"), sem("identities_made")
        block = ctx.enter_context(nc.Block())

        @block.sync
        def _(sp):
            sp.wait_ge(zeroed, len(zeros))
            for dst, src in loads:
                sp.dma_start(dst, src).then_inc(loaded, 16)
            sp.wait_ge(loaded, 16 * len(loads))

        @block.vector
        def _(dve):
            for z in zeros:
                dve.memset(z, 0.0).then_inc(zeroed, 1)

        @block.gpsimd
        def _(gp):
            gp.memset(ident, 0.0).then_inc(made, 1)
            gp.memset(identb, 0.0).then_inc(made, 1)
            gp.wait_ge(made, 2)
            gp.affine_select(out=ident, in_=ident, compare_op=ALU.not_equal, fill=1.0, base=0,
                             pattern=[[-1, P]], channel_multiplier=1)
            gp.affine_select(out=identb, in_=identb, compare_op=ALU.not_equal, fill=1.0, base=0,
                             pattern=[[-1, P]], channel_multiplier=1)
            gp.memset(small[:, 8:9], -0.5)


def build(nc, a, out, nb, n, stages=4):
    tiles = n // P
    adj = a["adj"]
    with ExitStack() as ctx:
        sb = lambda name, shape, dt=F32: ctx.enter_context(nc.sbuf_tensor(name, shape, dt))
        X = [sb("x_even", [P, nb * tiles * C]), sb("x_odd", [P, nb * tiles * C])]
        ident, identb, small = sb("ident", [P, P]), sb("identb", [P, P], BF16), sb("small", [P, 320])
        with ExitStack() as gat:
            sg = lambda name, shape, dt=F32: gat.enter_context(nc.sbuf_tensor(name, shape, dt))
            B2, A2 = sg("B2", [P, nb * n]), sg("A2", [P, nb * n // 2])
            TB = sg("TB", [P, nb * n])
            hidden = sg("hidden", [P, SLOTS, 4, n])
            adj_in, mask = sg("adj_in", [P, 2, n], I32), sg("mask", [P, 2, n])
            Z, PT = sg("Z", [P, n]), sg("PT", [P, n])
            work = hidden[:, 0, :, :].rearrange("p q n -> p (q n)")
            w_sel = [sg("w_sel0", [P, 62]), sg("w_sel1", [P, 62])]
            w_a, w_b = sg("w_a", [C, 2, P]), sg("w_b", [C, P])
            w_t, lin_w, lin_b, beta = sg("w_t", [C, P]), sg("lin_w", [C, C]), sg("lin_b", [P, C]), sg("beta", [P, 1])
            ycol = sg("ycol", [C, 1])

            xv = a["x"].rearrange("(t p) c -> p t c", p=P)
            loads = [(X[0][:, :].rearrange("p (t c) -> p t c", c=C), xv)]
            for i, name in enumerate(("L0_gnn_W2", "L1_gnn_yita")):
                loads += [(w_sel[i][0:C, 30:31], a[name]), (w_sel[i][C:P, 31:32], a[name])]
            loads += [(w_a[:, 0, 0:C], a["L0_aT"]), (w_a[:, 1, C:P], a["L0_aT"]),
                      (w_b[:, 0:C], a["L0_bT"]), (w_b[:, C:P], a["L0_bT"]),
                      (lin_w[:, :], a["L1_gnn_linWT"]), (lin_b[:, :], a["L1_gnn_linb"].to_broadcast([P, C])),
                      (beta[:, :], a["L1_gnn_beta"].to_broadcast([P, 1])), (ycol[:, :], a["L1_gnn_yita"])]
            load_constants(nc, a, loads, [w_sel[0][:, :], w_sel[1][:, :], w_a[:, :, :]], ident[:, :], identb[:, :], small)
            project_nodes(nc, X[0], None, "L0", w_a, w_b[:, :], None, X[0], B2, A2, None, work, ident[:, :], nb, n)
            additive_attention(nc, "L0", adj, X[0], X[1], B2, A2, None, w_sel[0], hidden, adj_in, mask, Z, PT,
                               small, ident[:, :], None, nb, n)
            layer1_constants(nc, [(w_a[:, 0, 0:C], a["L1_gnn_U2"]), (w_a[:, 1, C:P], a["L1_gnn_U2"]),
                                  (w_b[:, 0:C], a["L1_gnn_W2"]), (w_b[:, C:P], a["L1_gnn_W2"])],
                             w_sel[1], w_t, ycol, beta)
            project_nodes(nc, X[1], None, "L1", w_a, w_b[:, :], w_t[:, :], X[1], B2, A2, TB, work, ident[:, :], nb, n)
            additive_attention(nc, "L1", adj, X[1], X[0], B2, A2, TB, w_sel[1], hidden, adj_in, mask, Z, PT,
                               small, ident[:, :], dict(w=lin_w[:, :], bias=lin_b[:, :], beta1=beta[:, :]), nb, n)
        cur = 0
        if stages == 2:
            store_rows(nc, X[0], out, nb * tiles)
            return
        with ExitStack() as l2:
            sg = lambda name, shape, dt=F32: l2.enter_context(nc.sbuf_tensor(name, shape, dt))
            F2 = sg("F2", [P, n])
            F2B, F1, SEQ = sg("F2B", [P, nb * n]), sg("F1", [P, nb * tiles]), sg("SEQ", [P, nb * tiles * C])
            RET, work = sg("RET", [C, nb * n]), sg("work2", [P, 3072])
            adj_in, maskb = sg("adj_in2", [P, 2, n], I32), sg("maskb", [P, 2, n], BF16)
            U, Y = sg("U", [P, 2, n]), sg("Y", [P, 2, n])
            w1, b1col, b1row, a1 = sg("w1", [C, C]), sg("b1col", [C, 1]), sg("b1row", [P, 1, C]), sg("a1", [C, 1])
            a2 = sg("a2", [C, 1])
            a2B, ba1, ba2 = sg("a2B", [C, P]), sg("ba1", [P, 1]), sg("ba2", [P, 1])
            w = dict(W1=w1[:, :], b1col=b1col[:, :], b1row=b1row[:, :, :], a1=a1[:, :], a2B=a2B[:, :],
                     ba1=ba1[:, :], ba2=ba2[:, :])
            load_weights(nc, "w2", [(w1[:, :], a["L2_gnn_W1"]), (b1col[:, :], a["L2_b1col"]),
                              (b1row[:, 0, :], a["L2_b1row"].to_broadcast([P, C])), (a1[:, :], a["L2_a1col"]),
                              (a2[:, :], a["L2_a2col"]),
                              (ba1[:, :], a["L2_ba1"].to_broadcast([P, 1])),
                              (ba2[:, :], a["L2_ba2"].to_broadcast([P, 1]))],
                         [(a2B[:, :], a2[:, :].to_broadcast([C, P]))])
            project_layer2(nc, w, X[0], F2B, F1, SEQ, work, ident[:, :], nb, n)
            column_attention(nc, adj, F2B, F2, F1, SEQ, RET, adj_in, maskb, U, Y, small, identb[:, :], nb, n)
            finish_layer2(nc, RET, X[0], X[1], work, small, ident[:, :], nb, n)
        if stages == 3:
            store_rows(nc, X[1], out, nb * tiles)
            return
        with ExitStack() as l3:
            sg = lambda name, shape, dt=F32: l3.enter_context(nc.sbuf_tensor(name, shape, dt))
            buf = dict(K=sg("K", [P, PAIRS, n]), V=sg("V", [P, tiles, HEADS * C]), Q=sg("Q", [P, 2, PAIRS, P]),
                       xs=sg("xs", [P, tiles * C])[:, :], xT=sg("xT", [C, n])[:, :],
                       adj_in=sg("adj_in3", [P, 2, n], I32), maskf=sg("maskf", [P, n]), biased=sg("biased", [P, 2, n]),
                       Z=sg("Z3", [P, 4, n]), PT=sg("PT3", [P, 4, n]), rd=sg("rd", [P, 2, 2]),
                       rinv=sg("rinv", [P, 2, P]), R=sg("R", [P, P])[:, :], OT=sg("OT", [P, 2, PAIRS, P]),
                       y=sg("y3", [P, C])[:, :], yn=sg("yn", [P, 2, C]), small=small)
            wq, wk, wv, wp = sg("wq", [C, HEADS * C]), sg("wk", [C, HEADS * C]), sg("wv", [C, HEADS * C]), sg("wp", [P, PAIRS, C])
            bq, bk, bv, bp = sg("bq", [P, PAIRS, 1]), sg("bk", [P, PAIRS]), sg("bv", [P, HEADS * C]), sg("bp", [P, C])
            edge8 = sg("edge8", [P, EDGE_TYPES, HEADS])
            w = dict(Wq=wq[:, :], Wk=wk[:, :], Wv=wv[:, :], Wp=wp, bq=bq[:, :, :], bk=bk, bv=bv[:, :], bp=bp[:, :],
                     edge8=edge8[:, 1, :], scale=float(C) ** -0.5)
            load_weights(nc, "w3", [(wq[:, :], a["L3_gnn_Wq"]), (wk[:, :], a["L3_gnn_Wk"]), (wv[:, :], a["L3_gnn_Wv"]),
                              (wp[:, :, :], a["L3_gnn_Wp"].rearrange("(h p) c -> p h c", p=P)),
                              (bq[:, :, 0], a["L3_bqT"]), (bk[:, :], a["L3_bkT"]),
                              (bv[:, :], a["L3_bv"].to_broadcast([P, HEADS * C])),
                              (bp[:, :], a["L3_bp"].to_broadcast([P, C])),
                              (edge8[:, :, :].rearrange("p v h -> p (v h)"),
                               a["L3_edge"].to_broadcast([P, EDGE_TYPES * HEADS]))])
            scale_edge_bias(nc, edge8)
            multi_head_attention(nc, adj, out, w, X[1], buf, ident[:, :], nb, n)


def load_weights(nc, name, loads, spread=()):
    with ExitStack() as ctx:
        loaded = ctx.enter_context(nc.semaphore(name + "_loaded"))
        block = ctx.enter_context(nc.Block())

        @block.sync
        def _(sp):
            for dst, src in loads:
                sp.dma_start(dst, src).then_inc(loaded, 16)
            sp.wait_ge(loaded, 16 * len(loads))

        @block.vector
        def _(dve):
            dve.wait_ge(loaded, 16 * len(loads))
            for dst, src in spread:
                dve.tensor_copy(dst, src)


def scale_edge_bias(nc, edge8):
    with ExitStack() as ctx:
        block = ctx.enter_context(nc.Block())

        @block.vector
        def _(dve):
            dve.tensor_scalar(edge8[:, :, :], edge8[:, :, :], float(C) ** 0.5, None, ALU.mult)


def layer1_constants(nc, loads, w_sel, w_t, ycol, beta):
    with ExitStack() as ctx:
        loaded, scaled = ctx.enter_context(nc.semaphore("w1_loaded")), ctx.enter_context(nc.semaphore("w1_scaled"))
        block = ctx.enter_context(nc.Block())

        @block.sync
        def _(sp):
            for dst, src in loads:
                sp.dma_start(dst, src).then_inc(loaded, 16)
            sp.wait_ge(loaded, 16 * len(loads))

        @block.vector
        def _(dve):
            dve.tensor_scalar(w_sel[:, :], w_sel[:, :], 1.0 - GAT_SLOPE, None, ALU.mult)
            dve.memset(w_t[:, :], GAT_SLOPE).then_inc(scaled, 1)
            dve.wait_ge(scaled, 1)
            dve.tensor_scalar(w_t[:, :], w_t[:, :], ycol[:, :], None, ALU.mult)
            dve.tensor_scalar(beta[:, :], beta[:, :], 1.0, None, ALU.add)


def store_rows(nc, X, out, tiles):
    with ExitStack() as ctx:
        stored = ctx.enter_context(nc.semaphore("stored"))
        block = ctx.enter_context(nc.Block())

        @block.sync
        def _(sp):
            sp.dma_start(out.rearrange("(t p) c -> p t c", p=P),
                         X[:, :].rearrange("p (t c) -> p t c", c=C)).then_inc(stored, 16)
            sp.wait_ge(stored, 16)


def host_arrays(inputs):
    a = {k: np.ascontiguousarray(v) for k, v in inputs.items()}
    b, n, c = a["x"].shape
    r = {"x": a["x"].reshape(b * n, c), "adj": a["adj"].reshape(b * n, n)}
    w = a["L0_gnn_W1"]
    r["L0_aT"], r["L0_bT"] = np.ascontiguousarray(w[:, :c].T), np.ascontiguousarray(w[:, c:].T)
    r["L0_gnn_W2"] = a["L0_gnn_W2"].reshape(c, 1)
    r["L1_gnn_linWT"] = np.ascontiguousarray(a["L1_gnn_linW"].T)
    for k in ("L1_gnn_U2", "L1_gnn_W2", "L1_gnn_yita", "L1_gnn_beta"):
        r[k] = a[k]
    r["L2_gnn_W1"] = a["L2_gnn_W1"]
    r["L2_b1col"], r["L2_b1row"] = a["L2_gnn_b1"].reshape(c, 1), a["L2_gnn_b1"].reshape(1, c)
    r["L2_a1col"], r["L2_a2col"] = a["L2_gnn_a1"].reshape(c, 1), a["L2_gnn_a2"].reshape(c, 1)
    r["L2_ba1"], r["L2_ba2"] = a["L2_gnn_ba1"].reshape(1, 1), a["L2_gnn_ba2"].reshape(1, 1)
    for k in ("L3_gnn_Wq", "L3_gnn_Wk", "L3_gnn_Wv", "L3_gnn_Wp"):
        r[k] = a[k]
    r["L3_bqT"] = np.ascontiguousarray(a["L3_gnn_bq"].reshape(-1, P).T)
    r["L3_bkT"] = np.ascontiguousarray(a["L3_gnn_bk"].reshape(-1, P).T)
    r["L3_bv"], r["L3_bp"] = a["L3_gnn_bv"].reshape(1, -1), a["L3_gnn_bp"].reshape(1, -1)
    r["L3_edge"] = a["L3_gnn_edge_bias"].reshape(1, -1)
    r["L1_gnn_linb"] = a["L1_gnn_linb"].reshape(1, c)
    return r


def project_layer2(nc, w, X, F2B, F1, SEQ, work, ident, nb, n):
    tiles = n // P
    xs, xT, seqT = work[:, 0:tiles * C], work[0:C, 1024:1024 + n], work[0:C, 2048:2048 + n]
    with ExitStack() as ctx:
        sem = lambda s: ctx.enter_context(nc.semaphore("p2" + s))
        pX = ctx.enter_context(nc.psum_tensor("p2X", [C, n], F32))
        pT = ctx.enter_context(nc.psum_tensor("p2T", [C, n], F32))
        pF = ctx.enter_context(nc.psum_tensor("p2F", [P, n], F32))
        pS = ctx.enter_context(nc.psum_tensor("p2S", [P, tiles * C], F32))
        p1 = ctx.enter_context(nc.psum_tensor("p21", [P, HALF], F32))
        staged, transposed, xT_ready = sem("staged"), sem("transposed"), sem("xT_ready")
        seqT_made, seq_made, f_made = sem("seqT_made"), sem("seq_made"), sem("f_made")
        seqT_out, f2_out, seq_out, f1_out = sem("seqT_out"), sem("f2_out"), sem("seq_out"), sem("f1_out")
        block = ctx.enter_context(nc.Block())

        @block.scalar
        def _(act):
            with act.Fori(0, nb) as b:
                act.wait_ge(transposed, b)
                act.activation(xs, X[:, bass.ds(b * tiles * C, tiles * C)], ACT.Copy).then_inc(staged, 1)
                act.wait_ge(seqT_made, b + 1)
                act.wait_ge(f_made, b)
                act.activation(seqT, pT[:, :], ACT.Identity, bias=w["b1col"]).then_inc(seqT_out, 1)
                act.wait_ge(f_made, b + 1)
                act.activation(F2B[:, bass.ds(b * n, n)], pF[:, :], ACT.Identity, bias=w["ba2"]).then_inc(f2_out, 1)

        @block.vector
        def _(dve):
            with dve.Fori(0, nb) as b:
                dve.wait_ge(transposed, b + 1)
                dve.wait_ge(seq_made, b)
                dve.tensor_copy(xT, pX[:, :]).then_inc(xT_ready, 1)
                dve.wait_ge(seq_made, b + 1)
                dve.tensor_tensor(SEQ[:, bass.ds(b * tiles * C, tiles * C)].rearrange("p (t c) -> p t c", c=C),
                                  pS[:, :].rearrange("p (t c) -> p t c", c=C),
                                  w["b1row"].to_broadcast([P, tiles, C]), ALU.add).then_inc(seq_out, 1)
                dve.wait_ge(f_made, b + 1)
                dve.tensor_scalar(F1[:, bass.ds(b * tiles, tiles)], p1[:, 0:tiles], w["ba1"], None,
                                  ALU.add).then_inc(f1_out, 1)

        @block.tensor
        def _(pe):
            with pe.Fori(0, nb) as b:
                pe.wait_ge(staged, b + 1)
                pe.wait_ge(xT_ready, b)
                pe.nop(nofuse=True)
                for t in range(tiles):
                    last = pe.transpose(pX[:, t * P:(t + 1) * P], xs[:, t * C:(t + 1) * C], ident)
                last.then_inc(transposed, 1)
                pe.wait_ge(xT_ready, b + 1)
                pe.wait_ge(seqT_out, b)
                pe.nop(nofuse=True)
                for h in range(n // HALF):
                    last = pe.matmul(pT[:, h * HALF:(h + 1) * HALF], w["W1"], xT[:, h * HALF:(h + 1) * HALF],
                                     start=True, stop=True)
                last.then_inc(seqT_made, 1)
                pe.wait_ge(seq_out, b)
                for t in range(tiles):
                    last = pe.matmul(pS[:, t * C:(t + 1) * C], xT[:, t * P:(t + 1) * P], w["W1"],
                                     start=True, stop=True)
                last.then_inc(seq_made, 1)
                pe.wait_ge(seqT_out, b + 1)
                pe.wait_ge(f2_out, b)
                pe.wait_ge(f1_out, b)
                for h in range(n // HALF):
                    pe.matmul(pF[:, h * HALF:(h + 1) * HALF], w["a2B"], seqT[:, h * HALF:(h + 1) * HALF],
                              start=True, stop=True)
                for t in range(tiles):
                    last = pe.matmul(p1[:, t:t + 1], seqT[:, t * P:(t + 1) * P], w["a1"], start=True, stop=True)
                last.then_inc(f_made, 1)


def column_attention(nc, adj, F2B, F2, F1, SEQ, RET, adj_in, maskb, U, Y, small, identb, nb, n):
    tiles = n // P
    T = nb * tiles
    with ExitStack() as ctx:
        sem = lambda s: ctx.enter_context(nc.semaphore("c2" + s))
        pM = [ctx.enter_context(nc.psum_tensor(f"c2M{i}", [P, n], BF16)) for i in range(2)]
        pR = ctx.enter_context(nc.psum_tensor("c2R", [C, n], F32))
        adj_loaded = [sem(f"adj_loaded{i}") for i in range(2)]
        mask_ready, mask_turned, max_ready, shifted = (
            sem("mask_ready"), sem("mask_turned"), sem("max_ready"), sem("shifted"))
        leaky_ready, probs_ready, seq_scaled, summed, ret_out = (
            sem("leaky_ready"), sem("probs_ready"), sem("seq_scaled"), sem("summed"), sem("ret_out"))
        dve_step, inverted, f2_ready = sem("dve_step"), sem("inverted"), sem("f2_ready")
        col = lambda i, par: small[:, 16 + 2 * i + par:17 + 2 * i + par]
        scaled = [small[:, 64:128], small[:, 128:192]]
        block = ctx.enter_context(nc.Block())

        def pipeline(eng, stages):
            deepest = max(lag for lag, _ in stages)

            def at(b, j, first):
                for lag, what in stages:
                    if j >= lag:
                        what(b, j - lag, first and j == lag)
                    elif not first:
                        what(b - 1, j - lag + tiles, False)

            for j in range(tiles):
                at(0, j, True)
            if nb > 1:
                with eng.Fori(1, nb) as b:
                    for j in range(tiles):
                        at(b, j, False)
            for j in range(deepest):
                for lag, what in stages:
                    if j < lag:
                        what(nb - 1, j - lag + tiles, False)

        @block.sync
        def _(sp):
            def load(b, j, first):
                if not (isinstance(b, int) and b == 0 and j < 2):
                    sp.wait_ge(mask_ready, b * tiles + j - 1)
                sp.dma_start(adj_in[:, j % 2, :].rearrange("p (t c) -> p t c", c=P),
                             adj[bass.ds(b * n, n), j * P:(j + 1) * P].rearrange("(t p) c -> p t c", p=P)
                             ).then_inc(adj_loaded[j % 2], 16)
            pipeline(sp, [(0, load)])

        @block.gpsimd
        def _(gp):
            def make_mask(b, j, first):
                gp.wait_ge(adj_loaded[j % 2], 16 * (b * (tiles // 2) + j // 2 + 1))
                if not (isinstance(b, int) and b == 0 and j < 2):
                    gp.wait_ge(mask_turned, b * tiles + j - 1)
                gp.nop(nofuse=True)
                gp.tensor_scalar(maskb[:, j % 2, :], adj_in[:, j % 2, :], 0.0, NEG,
                                 ALU.is_le, ALU.mult).then_inc(mask_ready, 1)
            pipeline(gp, [(0, make_mask)])

        @block.tensor
        def _(pe):
            def turn(b, j, first):
                pe.wait_ge(mask_ready, b * tiles + j + 1)
                if not (isinstance(b, int) and b == 0 and j < 2):
                    pe.wait_ge(max_ready, b * tiles + j - 1)
                pe.nop(nofuse=True)
                for t in range(tiles):
                    last = pe.transpose(pM[j % 2][:, t * P:(t + 1) * P], maskb[:, j % 2, t * P:(t + 1) * P], identb)
                last.then_inc(mask_turned, 1)

            def weigh(b, j, first):
                pe.wait_ge(seq_scaled, b * tiles + j + 1)
                if j == 0:
                    pe.wait_ge(ret_out, b)
                for h in range(n // HALF):
                    last = pe.matmul(pR[:, h * HALF:(h + 1) * HALF], scaled[j % 2],
                                     Y[:, j % 2, h * HALF:(h + 1) * HALF], start=j == 0, stop=j == tiles - 1)
                last.then_inc(summed, 1)
            pipeline(pe, [(0, turn), (2, weigh)])

        @block.vector
        def _(dve):
            def masked_max(b, j, first):
                k, par = b * tiles + j, j % 2
                if j == 0:
                    dve.wait_ge(f2_ready, b + 1)
                dve.wait_ge(mask_turned, k + 1)
                if not (isinstance(b, int) and b == 0 and j < 2):
                    dve.wait_ge(shifted, k - 1)
                    dve.wait_ge(probs_ready, k - 1)
                dve.nop(nofuse=True)
                dve.tensor_tensor_reduce(out=U[:, par, :], in0=pM[par][:, :], in1=F2[:, :],
                                         scale=1.0, scalar=LOWEST, op0=ALU.add, op1=ALU.max,
                                         accum_out=col(0, par)).then_inc(max_ready, 1)
                dve.wait_ge(max_ready, k + 1)
                dve.tensor_tensor(col(1, par), col(0, par), F1[:, bass.ds(k, 1)], ALU.add).then_inc(dve_step, 1)
                dve.wait_ge(dve_step, dve_count(b, j, 0))
                dve.tensor_scalar(col(2, par), col(1, par), -L2_SLOPE, None, ALU.mult).then_inc(dve_step, 1)
                dve.wait_ge(dve_step, dve_count(b, j, 1))
                dve.scalar_tensor_tensor(out=col(3, par), in0=col(1, par), scalar=-1.0, in1=col(2, par),
                                         op0=ALU.mult, op1=ALU.min)

            def dve_count(b, j, i):
                return 2 * (b * tiles + j) + i + 1

            def leaky(b, j, first):
                k, par = b * tiles + j, j % 2
                dve.wait_ge(shifted, k + 1)
                dve.scalar_tensor_tensor(out=Y[:, par, :], in0=Y[:, par, :], scalar=L2_SLOPE, in1=Y[:, par, :],
                                         op0=ALU.mult, op1=ALU.max).then_inc(leaky_ready, 1)

            def scale_seq(b, j, first):
                k, par = b * tiles + j, j % 2
                dve.wait_ge(probs_ready, k + 1)
                if not (isinstance(b, int) and b == 0 and j < 2):
                    dve.wait_ge(summed, k - 1)
                dve.reciprocal(col(5, par), col(4, par)).then_inc(inverted, 1)
                dve.wait_ge(inverted, k + 1)
                dve.tensor_scalar(scaled[par], SEQ[:, bass.ds(k * C, C)], col(5, par), None,
                                  ALU.mult).then_inc(seq_scaled, 1)
            pipeline(dve, [(0, masked_max), (1, leaky), (2, scale_seq)])

        @block.scalar
        def _(act):
            def shift(b, j, first):
                k, par = b * tiles + j, j % 2
                act.wait_ge(max_ready, k + 1)
                if not (isinstance(b, int) and b == 0 and j < 2):
                    act.wait_ge(summed, k - 1)
                act.activation(Y[:, par, :], U[:, par, :], ACT.Identity,
                               bias=F1[:, bass.ds(k, 1)]).then_inc(shifted, 1)

            def exponentials(b, j, first):
                k, par = b * tiles + j, j % 2
                act.wait_ge(leaky_ready, k + 1)
                act.activation(Y[:, par, :], Y[:, par, :], ACT.Exp, bias=col(3, par),
                               accum_out=col(4, par)).then_inc(probs_ready, 1)

            def batch_f2(b, j, first):
                if j == 0:
                    act.wait_ge(max_ready, b * tiles)
                    act.activation(F2[:, :], F2B[:, bass.ds(b * n, n)], ACT.Copy).then_inc(f2_ready, 1)

            def evict(b, j, first):
                if j == tiles - 1:
                    act.wait_ge(summed, b * tiles + tiles)
                    act.activation(RET[:, bass.ds(b * n, n)], pR[:, :], ACT.Copy).then_inc(ret_out, 1)
            pipeline(act, [(0, batch_f2), (0, shift), (1, exponentials), (2, evict)])


def finish_layer2(nc, RET, X, XN, work, small, ident, nb, n):
    tiles = n // P
    neg, y = work[0:C, 0:n], work[:, 1024:1024 + tiles * C]
    stats = work[:, 1536:1536 + 6 * tiles].rearrange("p (t s) -> p t s", s=6)
    mv = work[:, 1600:1600 + 2 * tiles].rearrange("p (t s) -> p t s", s=2)
    vare, rstd, halfc = work[:, 1632:1640], work[:, 1640:1648], small[:, 8:9].to_broadcast([P, tiles])
    with ExitStack() as ctx:
        sem = lambda s: ctx.enter_context(nc.semaphore("f2" + s))
        pE = ctx.enter_context(nc.psum_tensor("f2E", [P, tiles * C], F32))
        neg_ready, exp_ready, elu_ready, turned = sem("neg_ready"), sem("exp_ready"), sem("elu_ready"), sem("turned")
        y_ready, stats_ready, var_ready, eps_added, rstd_ready, written = (
            sem("y_ready"), sem("stats_ready"), sem("var_ready"), sem("eps_added"), sem("rstd_ready"), sem("written"))
        block = ctx.enter_context(nc.Block())

        @block.scalar
        def _(act):
            with act.Fori(0, nb) as b:
                act.wait_ge(neg_ready, b + 1)
                act.activation(neg, neg, ACT.Exp).then_inc(exp_ready, 1)

        @block.tensor
        def _(pe):
            with pe.Fori(0, nb) as b:
                pe.wait_ge(elu_ready, b + 1)
                pe.nop(nofuse=True)
                for t in range(tiles):
                    last = pe.transpose(pE[:, t * C:(t + 1) * C], neg[:, t * P:(t + 1) * P], ident[0:C, 0:C])
                last.then_inc(turned, 1)

        @block.gpsimd
        def _(gp):
            with gp.Fori(0, nb) as b:
                gp.wait_ge(var_ready, b + 1)
                gp.nop(nofuse=True)
                gp.tensor_scalar(vare, mv[:, :, 1], EPS, 1.0, ALU.add, ALU.mult).then_inc(eps_added, 1)
                gp.wait_ge(eps_added, b + 1)
                gp.tensor_tensor(rstd, vare, halfc, ALU.pow).then_inc(rstd_ready, 1)

        @block.vector
        def _(dve):
            with dve.Fori(0, nb) as b:
                ret = RET[:, bass.ds(b * n, n)]
                dve.tensor_scalar(neg, ret, 0.0, None, ALU.min).then_inc(neg_ready, 1)
                dve.wait_ge(exp_ready, b + 1)
                dve.scalar_tensor_tensor(out=neg, in0=ret, scalar=0.0, in1=neg, op0=ALU.max,
                                         op1=ALU.add).then_inc(elu_ready, 1)
                dve.wait_ge(turned, b + 1)
                dve.scalar_tensor_tensor(out=y, in0=pE[:, :], scalar=-1.0, in1=X[:, bass.ds(b * tiles * C, tiles * C)],
                                         op0=ALU.add, op1=ALU.add).then_inc(y_ready, 1)
                dve.wait_ge(y_ready, b + 1)
                for t in range(tiles):
                    last = dve.bn_stats(stats[:, t, :], y[:, t * C:(t + 1) * C])
                last.then_inc(stats_ready, 1)
                dve.wait_ge(stats_ready, b + 1)
                dve.nop(nofuse=True)
                for t in range(tiles):
                    last = dve.bn_aggr(mv[:, t, :], stats[:, t, :])
                last.then_inc(var_ready, 1)
                dve.wait_ge(rstd_ready, b + 1)
                for t in range(tiles):
                    last = dve.tensor_scalar(XN[:, bass.ds((b * tiles + t) * C, C)], y[:, t * C:(t + 1) * C],
                                             mv[:, t, 0:1], rstd[:, t:t + 1], ALU.subtract, ALU.mult)
                last.then_inc(written, 1)


def kernel(**inputs):
    import concourse.bacc as bacc
    from concourse.bass_utils import run_bass_kernel_spmd

    nc = bacc.Bacc("TRN2", target_bir_lowering=False, num_devices=1)
    arrays = host_arrays(inputs)
    nb, n, _ = inputs["x"].shape
    args = {name: nc.dram_tensor(name, v.shape, mybir.dt.from_np(v.dtype), kind="ExternalInput").ap()
            for name, v in arrays.items()}
    out = nc.dram_tensor("out", (nb * n, C), F32, kind="ExternalOutput").ap()
    build(nc, args, out, nb, n)
    result = run_bass_kernel_spmd(nc, [arrays], core_ids=[0])
    return result.results[0]["out"].reshape(nb, n, C)
```
